# Optimizing a Trainium2 kernel written in Bass

```python
import numpy as np
import jax
import jax.numpy as jnp

def _softmax(x, axis=-1):
    return jax.nn.softmax(x, axis=axis)

def _gelu(x):
    return jax.nn.gelu(x, approximate=True)

def _silu(x):
    return jax.nn.silu(x)

def _sigmoid(x):
    return jax.nn.sigmoid(x)

def _layernorm(x, axis=-1, eps=1e-05):
    m = jnp.mean(x, axis=axis, keepdims=True)
    v = jnp.var(x, axis=axis, keepdims=True)
    return (x - m) / jnp.sqrt(v + eps)

def _scatter_add(tgt, idx, src, axis=0):
    return tgt.at[idx].add(src)

def _segment_sum(src, seg, n):
    return jax.ops.segment_sum(src, seg, n)
kernel_name = 'mk_gnn_preln_d4_gnn_r8_64db58'

def setup_inputs(seed: int=0):
    np.random.seed(seed)
    _w = jnp.asarray

    def _rec_inputs():
        import jax
        import jax.numpy as jnp
        _gk = jax.random.key(seed)
        x = -0.000202 + 1 * jax.random.normal(jax.random.fold_in(_gk, 1), (12500, 128), jnp.float32)
        src = jax.random.randint(jax.random.fold_in(_gk, 2), (200000,), 0, 12500, jnp.int32)
        dst = jnp.minimum((12500 * jax.random.uniform(jax.random.fold_in(_gk, 3), (200000,)) ** 2.0).astype(jnp.int32), 99999)
        _o = jnp.argsort(dst, stable=True)
        src = src[_o]
        dst = dst[_o]
        edge_weight = jax.random.uniform(jax.random.fold_in(_gk, 13), (200000,), jnp.float32, 0.0, 0.999998)
        node_vec1 = jax.random.uniform(jax.random.fold_in(_gk, 14), (12500, 1), jnp.float32, 0.0, 0.999994)
        return (x, src, dst, edge_weight, node_vec1)
    x, src, dst, edge_weight, node_vec1 = _rec_inputs()

    def _L0_gnn_setup():
        import jax, jax.numpy as jnp
        import numpy as np
        N_NODES = 6250

        def gcn_conv(x, W, b, src, dst, n_nodes):
            loop = jnp.arange(n_nodes, dtype=src.dtype)
            s = jnp.concatenate([src, loop])
            d = jnp.concatenate([dst, loop])
            deg = jax.ops.segment_sum(jnp.ones(d.shape[0], x.dtype), d, num_segments=n_nodes)
            dinv = jnp.where(deg > 0, jax.lax.rsqrt(deg), 0.0)
            h = x @ W
            norm = (dinv[s] * dinv[d])[:, None]
            msg = h[s] * norm
            out = jax.ops.segment_sum(msg, d, num_segments=n_nodes)
            return out + b
        key = jax.random.key(seed)
        k1, k2, k3, k4 = jax.random.split(key, 4)
        N, E, din, dh, dout = (N_NODES, 100000, 128, 256, 128)
        x = jax.random.normal(k1, (N, din), jnp.float32)
        edge_index = jax.random.randint(k2, (2, E), 0, N, jnp.int64)
        W1 = jax.random.normal(k3, (din, dh), jnp.float32) / np.sqrt(din)
        b1 = jnp.zeros((dh,), jnp.float32)
        W2 = jax.random.normal(k4, (dh, dout), jnp.float32) / np.sqrt(dh)
        b2 = jnp.zeros((dout,), jnp.float32)
        return {'x': x, 'edge_index': edge_index, 'W1': W1, 'b1': b1, 'W2': W2, 'b2': b2}
    _L0_gnn_all = _L0_gnn_setup()
    _L0_gnn_in = {k: v for k, v in _L0_gnn_all.items() if k in ('W1', 'b1', 'W2', 'b2')}
    del _L0_gnn_all

    def _L1_gnn_setup():
        import jax, jax.numpy as jnp
        import numpy as np
        EPS = 1e-12
        key = jax.random.key(seed)
        k1, k2, k3, k4, k5 = jax.random.split(key, 5)
        N, E, D_IN, D_OUT = (12500, 200000, 128, 128)
        features = jax.random.normal(k1, (N, D_IN), dtype=jnp.float32)
        W = jax.random.normal(k2, (D_OUT, D_IN), dtype=jnp.float32) * 0.05
        b = jax.random.normal(k3, (D_OUT,), dtype=jnp.float32) * 0.05
        src = jax.random.randint(k4, (E,), 0, N, dtype=jnp.int32)
        dst = jax.random.randint(k5, (E,), 0, N, dtype=jnp.int32)
        return {'features': features, 'W': W, 'b': b, 'src': src, 'dst': dst}
    _L1_gnn_all = _L1_gnn_setup()
    _L1_gnn_in = {k: v for k, v in _L1_gnn_all.items() if k in ('W', 'b')}
    del _L1_gnn_all

    def _L2_gnn_setup():
        import jax, jax.numpy as jnp
        import numpy as np
        N_NODES = 6250
        N_EDGES = 75000
        D_IN = 128
        D_OUT = 128
        key = jax.random.key(seed)
        k1, k2, k3, k4 = jax.random.split(key, 4)
        x = jax.random.normal(k1, (N_NODES, D_IN), dtype=jnp.float32)
        edge_index = jax.random.randint(k2, (2, N_EDGES), 0, N_NODES, dtype=jnp.int64)
        edge_attr = jax.random.uniform(k3, (N_EDGES,), dtype=jnp.float32)
        W = jax.random.normal(k4, (D_OUT, D_IN), dtype=jnp.float32) / np.sqrt(D_IN)
        b = jnp.zeros((D_OUT,), dtype=jnp.float32)
        return {'x': x, 'edge_index': edge_index, 'edge_attr': edge_attr, 'W': W, 'b': b}
    _L2_gnn_all = _L2_gnn_setup()
    _L2_gnn_in = {k: v for k, v in _L2_gnn_all.items() if k in ('W', 'b')}
    del _L2_gnn_all

    def _L3_gnn_setup():
        import jax, jax.numpy as jnp
        import numpy as np
        EPS = 1e-05

        def _bn(x, gamma, beta):
            mean = x.mean(axis=0, keepdims=True)
            var = x.var(axis=0, keepdims=True)
            return (x - mean) * jax.lax.rsqrt(var + EPS) * gamma + beta

        def _silu(x):
            return x * jax.nn.sigmoid(x)
        N, E, H, NH = (6250, 100000, 128, 4)
        HD = H // NH
        key = jax.random.key(seed)
        ks = jax.random.split(key, 8)
        x = jax.random.normal(ks[0], (N, H), dtype=jnp.float32)
        weight = jax.random.uniform(ks[1], (N, 1), dtype=jnp.float32)
        src = jax.random.randint(ks[2], (E,), 0, N)
        dst = jax.random.randint(ks[3], (E,), 0, N)
        Wf = jax.random.normal(ks[4], (2 * H, 1), dtype=jnp.float32) * 0.05
        bf = jnp.zeros((1,), jnp.float32)
        f_gamma = jnp.ones((1,), jnp.float32)
        f_beta = jnp.zeros((1,), jnp.float32)
        Wg = jax.random.normal(ks[5], (NH, 2 * H, HD), dtype=jnp.float32) * 0.05
        bg = jnp.zeros((NH, HD), jnp.float32)
        g_gamma = jnp.ones((NH, HD), jnp.float32)
        g_beta = jnp.zeros((NH, HD), jnp.float32)
        n_gamma = jnp.ones((H,), jnp.float32)
        n_beta = jnp.zeros((H,), jnp.float32)
        return dict(x=x, weight=weight, src=src, dst=dst, Wf=Wf, bf=bf, f_gamma=f_gamma, f_beta=f_beta, Wg=Wg, bg=bg, g_gamma=g_gamma, g_beta=g_beta, n_gamma=n_gamma, n_beta=n_beta)
    _L3_gnn_all = _L3_gnn_setup()
    _L3_gnn_in = {k: v for k, v in _L3_gnn_all.items() if k in ('Wf', 'bf', 'f_gamma', 'f_beta', 'Wg', 'bg', 'g_gamma', 'g_beta', 'n_gamma', 'n_beta')}
    del _L3_gnn_all
    return {'x': x, 'src': src, 'dst': dst, 'edge_weight': edge_weight, 'node_vec1': node_vec1, 'L0_gnn_W1': _L0_gnn_in['W1'], 'L0_gnn_b1': _L0_gnn_in['b1'], 'L0_gnn_W2': _L0_gnn_in['W2'], 'L0_gnn_b2': _L0_gnn_in['b2'], 'L1_gnn_W': _L1_gnn_in['W'], 'L1_gnn_b': _L1_gnn_in['b'], 'L2_gnn_W': _L2_gnn_in['W'], 'L2_gnn_b': _L2_gnn_in['b'], 'L3_gnn_Wf': _L3_gnn_in['Wf'], 'L3_gnn_bf': _L3_gnn_in['bf'], 'L3_gnn_f_gamma': _L3_gnn_in['f_gamma'], 'L3_gnn_f_beta': _L3_gnn_in['f_beta'], 'L3_gnn_Wg': _L3_gnn_in['Wg'], 'L3_gnn_bg': _L3_gnn_in['bg'], 'L3_gnn_g_gamma': _L3_gnn_in['g_gamma'], 'L3_gnn_g_beta': _L3_gnn_in['g_beta'], 'L3_gnn_n_gamma': _L3_gnn_in['n_gamma'], 'L3_gnn_n_beta': _L3_gnn_in['n_beta']}

def reference(x, src, dst, edge_weight, node_vec1, L0_gnn_W1, L0_gnn_b1, L0_gnn_W2, L0_gnn_b2, L1_gnn_W, L1_gnn_b, L2_gnn_W, L2_gnn_b, L3_gnn_Wf, L3_gnn_bf, L3_gnn_f_gamma, L3_gnn_f_beta, L3_gnn_Wg, L3_gnn_bg, L3_gnn_g_gamma, L3_gnn_g_beta, L3_gnn_n_gamma, L3_gnn_n_beta):
    import jax
    import jax.numpy as jnp

    def _L0_gnn_ref(x, edge_index, W1, b1, W2, b2):
        import jax, jax.numpy as jnp
        import numpy as np
        N_NODES = 6250

        def gcn_conv(x, W, b, src, dst, n_nodes):
            loop = jnp.arange(n_nodes, dtype=src.dtype)
            s = jnp.concatenate([src, loop])
            d = jnp.concatenate([dst, loop])
            deg = jax.ops.segment_sum(jnp.ones(d.shape[0], x.dtype), d, num_segments=n_nodes)
            dinv = jnp.where(deg > 0, jax.lax.rsqrt(deg), 0.0)
            h = x @ W
            norm = (dinv[s] * dinv[d])[:, None]
            msg = h[s] * norm
            out = jax.ops.segment_sum(msg, d, num_segments=n_nodes)
            return out + b
        src, dst = (edge_index[0], edge_index[1])
        n = x.shape[0]
        h = jax.nn.relu(gcn_conv(x, W1, b1, src, dst, n))
        return gcn_conv(h, W2, b2, src, dst, n)

    def _L1_gnn_ref(features, W, b, src, dst):
        import jax, jax.numpy as jnp
        import numpy as np
        EPS = 1e-12
        N = features.shape[0]
        neigh_sum = jax.ops.segment_sum(features[src], dst, num_segments=N)
        total = jnp.sum(features, axis=0)
        h_NN = total[None, :] - neigh_sum
        norm = jnp.sqrt(jnp.sum(h_NN * h_NN, axis=1, keepdims=True))
        h_norm = h_NN / jnp.maximum(norm, EPS)
        return h_norm @ W.T + b

    def _L2_gnn_ref(x, edge_index, edge_attr, W, b):
        import jax, jax.numpy as jnp
        import numpy as np
        N_NODES = 6250
        N_EDGES = 75000
        D_IN = 128
        D_OUT = 128
        N = x.shape[0]
        loop = jnp.arange(N, dtype=edge_index.dtype)
        row = jnp.concatenate([edge_index[0], loop])
        col = jnp.concatenate([edge_index[1], loop])
        w = jnp.concatenate([edge_attr, jnp.ones((N,), dtype=x.dtype)])
        deg = jax.ops.segment_sum(w, col, num_segments=N)
        dinv_sqrt = jnp.where(deg > 0, jax.lax.rsqrt(deg), 0.0)
        norm = dinv_sqrt[row] * w * dinv_sqrt[col]
        x_lin = x @ W.T
        msg = x_lin[row] * norm[:, None]
        out = jax.ops.segment_sum(msg, col, num_segments=N)
        return out + b

    def _L3_gnn_ref(x, weight, src, dst, Wf, bf, f_gamma, f_beta, Wg, bg, g_gamma, g_beta, n_gamma, n_beta):
        import jax, jax.numpy as jnp
        import numpy as np
        EPS = 1e-05

        def _bn(x, gamma, beta):
            mean = x.mean(axis=0, keepdims=True)
            var = x.var(axis=0, keepdims=True)
            return (x - mean) * jax.lax.rsqrt(var + EPS) * gamma + beta

        def _silu(x):
            return x * jax.nn.sigmoid(x)
        N = x.shape[0]
        E = src.shape[0]
        hihj = jnp.concatenate([x[src], x[dst]], axis=-1)
        exp_e = jnp.exp(_silu(_bn(hihj @ Wf + bf, f_gamma, f_beta)))
        we = weight[src] * exp_e
        sum_w_exp = jax.ops.segment_sum(we, dst, num_segments=N)
        a = we / sum_w_exp[dst]
        z = jnp.einsum('ed,hdk->ehk', hihj, Wg) + bg
        z = _silu(_bn(z, g_gamma, g_beta))
        msg = (a[:, :, None] * z).reshape(E, -1)
        h = jax.ops.segment_sum(msg, dst, num_segments=N)
        out = _bn(h, n_gamma, n_beta) + x
        return out
    edge_index = jnp.stack([src, dst])
    h = jnp.maximum(_layernorm(x, axis=-1), 0.0)
    x = x + _L0_gnn_ref(h, edge_index, L0_gnn_W1, L0_gnn_b1, L0_gnn_W2, L0_gnn_b2)
    h = jnp.maximum(_layernorm(x, axis=-1), 0.0)
    x = x + _L1_gnn_ref(h, L1_gnn_W, L1_gnn_b, src, dst)
    h = jnp.maximum(_layernorm(x, axis=-1), 0.0)
    x = x + _L2_gnn_ref(h, edge_index, edge_weight, L2_gnn_W, L2_gnn_b)
    h = jnp.maximum(_layernorm(x, axis=-1), 0.0)
    x = x + _L3_gnn_ref(h, node_vec1, src, dst, L3_gnn_Wf, L3_gnn_bf, L3_gnn_f_gamma, L3_gnn_f_beta, L3_gnn_Wg, L3_gnn_bg, L3_gnn_g_gamma, L3_gnn_g_beta, L3_gnn_n_gamma, L3_gnn_n_beta)
    return x

_drawn_inputs = setup_inputs


def setup_inputs(seed=0):
    import zlib

    import numpy as np

    out = dict(_drawn_inputs(seed))
    spreads = {'L0_gnn_b1': (0.0, 0.1),
     'L0_gnn_b2': (0.0, 0.1),
     'L2_gnn_b': (0.0, 0.1),
     'L3_gnn_bg': (0.0, 0.8),
     'L3_gnn_g_gamma': (1.0, 0.6),
     'L3_gnn_g_beta': (0.0, 0.587),
     'L3_gnn_n_gamma': (1.0, 0.2),
     'L3_gnn_n_beta': (0.0, 0.1)}
    factors = {}
    for name, (base, spread) in spreads.items():
        noise = np.random.default_rng([zlib.crc32(name.encode()), seed]).standard_normal(out[name].shape)
        drawn = base * np.exp(spread * noise) if base else spread * noise
        out[name] = jnp.asarray(drawn.astype(out[name].dtype))
    for name, factor in factors.items():
        out[name] = (out[name] * factor).astype(out[name].dtype)
    return out
```

```python
from contextlib import ExitStack

import concourse.bass as bass
import concourse.mybir as mybir

P = 128
F = 128
HALF = 16
BODY = 2 * HALF
CW = 7
ACW = F + 2
PSLOTS = 4
LN_EPS = 1e-5
NORM_EPS = 1e-12
BN_EPS = 1e-5
TINY = 1e-30


class Steps:

    def __init__(self, eng, sem, start, per_round):
        self.eng, self.sem, self.start, self.n, self.per_round = eng, sem, start, 0, per_round

    def __call__(self, ins):
        self.n += 1
        ins.then_inc(self.sem, 1)
        self.eng.wait_ge(self.sem, self.start + self.n)

    def end(self):
        assert self.n == self.per_round, self.n


def gnn_kernel(nc, x, src, dst, edge_weight, node_vec1, L0_W1, L0_b1, L0_W2, L0_b2, L1_W, L1_b, L2_W, L2_b,
               Wf, bf, f_gamma, f_beta, Wg, bg, g_gamma, g_beta, n_gamma, n_beta, out):
    f32, i32, i16 = mybir.dt.float32, mybir.dt.int32, mybir.dt.int16
    ALU, ACT, AX = mybir.AluOpType, mybir.ActivationFunctionType, mybir.AxisListType
    DVE, PE = mybir.EngineType.DVE, mybir.EngineType.PE

    N, E = x.shape[0], src.shape[0]
    HID = L0_W1.shape[1]
    HM = HID // P
    NH, HD = bg.shape
    NW = -(-N // P)
    NT = -(-E // P)
    ROUNDS = -(-(NT + NW) // BODY)
    NI = ROUNDS * BODY
    HALVES = 2 * ROUNDS
    TROWS = NI - NW
    NTAB = NI + BODY
    CHUNKS = NW // CW
    assert CHUNKS * CW == NW and NI % P == 0 and TROWS >= NT
    IG = NI // P
    NPAD = NW * P
    TAIL = N - (NW - 1) * P
    ETAIL = E - (NT - 1) * P
    FAR = 1 << 20
    CC = CW * F
    SCW = F + 1

    ctx = ExitStack()
    with ctx:
        def sb(name, shape, dt=f32):
            return ctx.enter_context(nc.sbuf_tensor(name, shape, dt))

        def sem(name):
            return ctx.enter_context(nc.semaphore(name))

        def dram(name, shape, dt=f32):
            return nc.dram_tensor(name, shape, dt, kind="Internal").ap()

        ctx.enter_context(nc.allow_non_contiguous_dma(reason="strided columns of small vectors"))

        src_rows = dram("src_rows", [TROWS, P], i32)
        dst_rows = dram("dst_rows", [TROWS, P], i32)
        ew_rows = dram("ew_rows", [TROWS, P])
        table = dram("table", [NPAD, F])
        ptable = dram("ptable", [NPAD, ACW])
        zrows = dram("zrows", [HALVES, P, HALF * ACW])
        item_win = dram("item_win", [NI], i16)
        dl_rows = dram("dl_rows", [NTAB, P])

        xs = sb("xs", [P, NW, F])
        acc = sb("acc", [P, NW + 1, ACW])
        acc_flat = acc[:].rearrange("p w f -> p (w f)")
        ring = sb("ring", [P, BODY, ACW])
        ring_n = ring[:].rearrange("p u f -> p (u f)")[:, 0:BODY * F].rearrange("p (u f) -> p u f", f=F)
        onehot = sb("onehot", [P, BODY, P])
        work = sb("work", [P, 4, CC])
        zbuf = sb("zbuf", [P, HALF, ACW + SCW])
        src_tab = sb("src_tab", [P, NTAB], i16)
        dl_tab = sb("dl_tab", [P, NTAB])
        ew_tab = sb("ew_tab", [P, NTAB])
        win_tab = sb("win_tab", [1, NI], i16)
        idx_stage = sb("idx_stage", [P, 2, HALF], i32)
        ident = sb("ident", [P, P])
        ones = sb("ones", [P, P])
        iota_col = sb("iota_col", [P, P])
        iota_row = sb("iota_row", [P, 1])
        node_id = sb("node_id", [P, NW + 1])
        is_node = sb("is_node", [P, NW])
        no_edges = sb("no_edges", [P, NW])
        dinv = sb("dinv", [P, NW])
        dinv2 = sb("dinv2", [P, NW])
        node_w = sb("node_w", [P, NW])
        w1 = sb("w1", [P, HID])
        w2 = sb("w2", [P, HM, F])
        w_l1 = sb("w_l1", [P, F])
        w_l2 = sb("w_l2", [P, F])
        w_z = sb("w_z", [P, 2, SCW])
        b1c = sb("b1c", [P, HM])
        rows = sb("rows", [1, 12, SCW])
        B2, BL1, BL2, BGF, GAMMA, BETA, NGAMMA, NBETA, RT0, RT1, RT2, RT3 = range(12)
        wide = sb("wide", [P, 4, SCW])
        eps_ln = sb("eps_ln", [P, 1])
        small = sb("small", [P, 14, NW + 1])
        stats = sb("stats", [P, CW, 6])
        mv = sb("mv", [P, CW, 2])
        sc16 = sb("sc16", [P, 8, HALF])

        bank = [ctx.enter_context(nc.psum_tensor(f"bank{b}", [P, 512], f32)) for b in range(8)]

        gathered = [sem(f"gathered{u}") for u in range(BODY)]
        gathers = [CHUNKS // 2] * (2 * CW) + [IG] * 3 + [0] * (BODY - 2 * CW - 3)
        s_staged = sem("idx_staged")
        s_onehot = sem("onehot_built")
        s_prod = sem("product_done")
        s_added = sem("product_added")
        s_tick = sem("tick")

        def dyn(ap, start, n):
            return ap[:, bass.ds(start, n)]

        def windows(ap, w, n=1):
            return ap[:, bass.ds(w, n), 0:F]

        def node_rows(tab, c):
            return tab[bass.ds(c * CW * P, CW * P), :].rearrange("(w p) f -> p w f", p=P)

        def over_f(ap, n=CW):
            return ap.unsqueeze(2).to_broadcast([P, n, F])

        def over_w(ap, n=CW):
            return ap.unsqueeze(1).to_broadcast([P, n, F])

        def chunk(ap):
            return ap.rearrange("p (w f) -> p w f", f=F)

        s_const, s_pad, s_rows, s_last, s_weights, s_x = (sem(n) for n in (
            "const", "pad", "rows_copied", "last_loaded", "weights", "x_loaded"))
        s_lastb, s_lastc, s_dve, s_cnt, s_pe = (sem(n) for n in (
            "last_wide", "last_kept", "setup_dve", "rooted", "setup_pe"))
        s_wout, s_win, s_act = (sem(n) for n in ("win_out", "win_in", "setup_act"))
        s_dlrow, s_tr, s_kept, s_dlout = (sem(n) for n in ("dl_row", "transposed", "tables_kept", "dl_out"))

        onehot_flat = onehot[:].rearrange("p u f -> p (u f)")
        last_b = onehot_flat[:, 0:TROWS // 2 + 1].bitcast(i16)[:, 0:TROWS]
        junk16 = onehot_flat[:, TROWS:TROWS + TROWS // 2 + 1].bitcast(i16)[:, 0:TROWS]
        last_i = zbuf[:].rearrange("p u f -> p (u f)")[0:1, 0:TROWS].bitcast(i32)
        last_f = zbuf[:].rearrange("p u f -> p (u f)")[0:1, TROWS:2 * TROWS]
        wload = work[:, 0, 0:2 * F].rearrange("p (a f) -> p a f", a=2)
        shift = work[:, 1, 0:P]
        wrap = work[:, 1, P:2 * P]
        first = work[:, 1, 2 * P:3 * P]
        pads = work[:, 1, 3 * P:5 * P]
        tile_cnt, row_ptr, bound, item_id, item_w, item_w128, wplus1 = (small[:, k, :] for k in range(7))
        tile_idx = small[:, 7, 0:2 * CW].bitcast(i32)
        in_tile = small[:, 8, 0:2 * CW]
        item_t = small[:, 9, 0:IG].bitcast(i32)
        item_off = small[:, 10, 0:IG // 2 + 1].bitcast(i16)[:, 0:IG]
        deg = small[:, 11, 0:NW]
        deg_r = small[:, 12, 0:NW]
        tcol = small[:, 13, 0:1].bitcast(i32)
        no_dst = work[0:BODY, 0, 2 * F:3 * F]
        found = ring[:].rearrange("p u f -> p (u f)")[:, 0:2 * CC].rearrange("p (b k f) -> p b k f", b=2, f=F)
        found_i = found.bitcast(i32)
        lower = work[:, 2:4, :].rearrange("p b (k f) -> p b k f", f=F)
        got = ring[:, 0:3, 0:P]
        got_f = work[:, 2, 0:2 * P].rearrange("p (a f) -> p a f", a=2)
        le = work[:, 2:4, :].rearrange("p b c -> p (b c)")[:, 0:IG * NW].rearrange("p (g w) -> p g w", g=IG)

        SEARCH = 2 * (CW + 1) + 2 * 4
        SEARCHED = 1 + SEARCH * (CHUNKS // 2)
        MERGED = SEARCHED + 7

        with nc.Block() as block:
            @block.gpsimd
            def _(pool):
                nc.gpsimd.memset(pads.bitcast(i32)[:, 0:P], 0)
                nc.gpsimd.memset(pads.bitcast(i32)[:, P:2 * P], FAR).then_inc(s_pad, 1)
                nc.gpsimd.memset(xs[:, NW - 1, :], 0.0).then_inc(s_pad, 1)
                nc.gpsimd.memset(node_w[:], 0.0).then_inc(s_pad, 1)
                for m in (ident[:], shift, wrap, first):
                    nc.gpsimd.memset(m, 0.0).then_inc(s_act, 1)
                nc.gpsimd.memset(ones[:], 1.0)
                nc.gpsimd.memset(eps_ln[:], LN_EPS)
                pool.wait_ge(s_act, 4)
                for m, base, step, cm in ((ident[:], 0, -1, 1), (shift, -1, -1, 1), (wrap, P - 1, -1, P), (first, 0, 0, 1)):
                    nc.gpsimd.affine_select(out=m, in_=m, compare_op=ALU.not_equal, fill=1.0, base=base,
                                            pattern=[[step, P]], channel_multiplier=cm)
                kw = dict(allow_small_or_imprecise_dtypes=True)
                nc.gpsimd.iota(iota_col[:], [[1, P]], base=0, channel_multiplier=0, **kw)
                nc.gpsimd.iota(iota_row[:], [[0, 1]], base=0, channel_multiplier=1, **kw)
                nc.gpsimd.iota(node_id[:], [[P, NW + 1]], base=0, channel_multiplier=1, **kw)
                nc.gpsimd.iota(item_id[:, 0:IG], [[P, IG]], base=0, channel_multiplier=1, **kw)
                nc.gpsimd.iota(wplus1[:, 0:NW], [[1, NW]], base=1, channel_multiplier=0, **kw).then_inc(s_const, 1)
                with pool.Fori(0, CHUNKS // 2) as i:
                    for b in range(2):
                        pool.wait_ge(s_dve, 1 + SEARCH * i + (b + 1) * (CW + 1))
                        pool.sem_inc(s_act, 1)
                        for k in range(CW):
                            pool.indirect_dma_start(
                                out=found_i[:, b, k, :], out_offset=None, in_=dst_rows,
                                in_offset=bass.IndirectOffsetOnAxis(ap=tile_idx[:, b * CW + k:b * CW + k + 1], axis=0),
                            ).then_inc(gathered[b * CW + k], 16)
                with pool.Fori(0, IG) as g:
                    pool.wait_ge(s_dve, MERGED + 2 * g + 1)
                    pool.sem_inc(s_act, 1)
                    for k, rows_of in enumerate((src_rows, dst_rows, ew_rows)):
                        o = got[:, k, :]
                        pool.indirect_dma_start(
                            out=o if k == 2 else o.bitcast(i32), out_offset=None, in_=rows_of,
                            in_offset=bass.IndirectOffsetOnAxis(ap=tcol, axis=0)).then_inc(gathered[2 * CW + k], 16)

            @block.sync
            def _(sp):
                sp.sem_inc(s_dlout, 16)
                sp.wait_ge(s_pad, 3)
                full = (NT - 1) * P
                for rows_of, a, pad in ((dst_rows, dst, pads.bitcast(i32)[:, P:2 * P]), (src_rows, src, pads.bitcast(i32)[:, 0:P]),
                                        (ew_rows, edge_weight, pads[:, 0:P])):
                    sp.dma_start(rows_of[0:NT - 1, :], a[0:full].rearrange("(t e) -> t e", e=P)).then_inc(s_rows, 16)
                    sp.dma_start(rows_of[NT - 1:NT, 0:ETAIL], a[full:E].rearrange("(t e) -> t e", t=1)).then_inc(s_rows, 16)
                    if ETAIL < P:
                        sp.dma_start(rows_of[NT - 1:NT, ETAIL:P], pad[0:1, ETAIL:P]).then_inc(s_rows, 16)
                    else:
                        sp.dma_start(rows_of[NT:NT + 1, :], pad[0:1, :]).then_inc(s_rows, 16)
                    sp.dma_start(rows_of[NT:TROWS, :], pad[0:TROWS - NT, :]).then_inc(s_rows, 16)
                sp.wait_ge(s_rows, 12 * 16)
                sp.dma_start(last_i, dst_rows[:, P - 1:P].rearrange("t o -> o t")).then_inc(s_last, 16)
                sp.wait_ge(s_wout, 1)
                sp.dma_start(item_win.rearrange("(g p) -> p g", p=P), item_off).then_inc(s_win, 16)
                sp.wait_ge(s_win, 16)
                sp.dma_start(win_tab[:], item_win.rearrange("(o i) -> o i", o=1)).then_inc(s_win, 16)
                sp.wait_ge(s_added, PSLOTS)
                sp.dma_start(dl_rows[NI:NTAB, :], no_dst).then_inc(s_win, 16)
                with sp.Fori(0, IG) as g:
                    sp.wait_ge(s_dlrow, g + 1)
                    sp.sem_inc(s_tick, 1)
                    sp.dma_start(dl_rows[bass.ds(g * P, P), :], got_f[:, 1, :]).then_inc(s_dlout, 16)
                sp.wait_ge(s_win, 48)
                sp.wait_ge(s_dlout, 16 * IG + 16)

            @block.scalar
            def _(act):
                act.wait_ge(s_pad, 3)
                act.dma_start(xs[:, 0:NW - 1, :], x[0:(NW - 1) * P, :].rearrange("(w p) f -> p w f", p=P)).then_inc(s_x, 16)
                act.dma_start(xs[0:TAIL, NW - 1, :], x[(NW - 1) * P:N, :]).then_inc(s_x, 16)
                loads = [
                    (w1[:], L0_W1), (w2[:], L0_W2.rearrange("(m p) f -> p m f", p=P)),
                    (wload[:, 0, :], L1_W), (wload[:, 1, :], L2_W), (b1c[:], L0_b1.rearrange("(m p) -> p m", p=P)),
                    (rows[:, B2, 0:F], L0_b2.rearrange("(o f) -> o f", o=1)),
                    (rows[:, BL1, 0:F], L1_b.rearrange("(o f) -> o f", o=1)),
                    (rows[:, BL2, 0:F], L2_b.rearrange("(o f) -> o f", o=1)),
                    (rows[:, BGF, 0:F], bg.rearrange("(o h) k -> o (h k)", o=1)),
                    (rows[:, BGF, F:SCW], bf.rearrange("(o f) -> o f", o=1)),
                    (rows[:, GAMMA, 0:F], g_gamma.rearrange("(o h) k -> o (h k)", o=1)),
                    (rows[:, GAMMA, F:SCW], f_gamma.rearrange("(o f) -> o f", o=1)),
                    (rows[:, BETA, 0:F], g_beta.rearrange("(o h) k -> o (h k)", o=1)),
                    (rows[:, BETA, F:SCW], f_beta.rearrange("(o f) -> o f", o=1)),
                    (rows[:, NGAMMA, 0:F], n_gamma.rearrange("(o f) -> o f", o=1)),
                    (rows[:, NBETA, 0:F], n_beta.rearrange("(o f) -> o f", o=1)),
                    (node_w[:, 0:NW - 1], node_vec1[0:(NW - 1) * P, :].rearrange("(w p) o -> p (w o)", p=P)),
                    (node_w[0:TAIL, NW - 1:NW], node_vec1[(NW - 1) * P:N, :]),
                ]
                for part in range(2):
                    loads.append((w_z[:, part, 0:F].rearrange("p (h k) -> p h k", h=NH),
                                  Wg[:, part * F:(part + 1) * F, :].rearrange("h d k -> d h k")))
                    loads.append((w_z[:, part, F:SCW], Wf[part * F:(part + 1) * F, :]))
                for to, of in loads:
                    act.dma_start(to, of).then_inc(s_weights, 16)
                act.wait_ge(s_weights, 16 * len(loads))
                act.wait_ge(s_x, 32)
                act.wait_ge(s_pe, 1)
                nc.scalar.copy(w_l1[:], bank[6][:, 0:F])
                nc.scalar.copy(w_l2[:], bank[6][:, F:2 * F])
                act.wait_ge(s_dve, SEARCHED + 3)
                nc.scalar.activation(deg_r, deg, ACT.Sqrt).then_inc(s_cnt, 1)
                with act.Fori(0, IG) as g:
                    act.wait_ge(gathered[2 * CW], 16 * g + 16)
                    nc.scalar.copy(got_f[:, 0, :], got[:, 0, :].bitcast(i32)).then_inc(s_kept, 1)
                    act.wait_ge(s_tr, g + 1)
                    nc.scalar.copy(dyn(src_tab, g * P, P), bank[0][:, 0:P])
                    nc.scalar.copy(dyn(ew_tab, g * P, P), bank[0][:, 2 * P:3 * P]).then_inc(s_kept, 1)

            @block.vector
            def _(dve):
                nc.vector.memset(src_tab[:, NI:NTAB], 0)
                nc.vector.memset(dl_tab[:, NI:NTAB], -1.0)
                nc.vector.memset(ew_tab[:, NI:NTAB], 0.0)
                nc.vector.memset(acc[:, :, 0:F], 0.0)
                nc.vector.memset(acc[:, :, F:F + 1], 1.0)
                nc.vector.memset(acc[:, :, F + 1:ACW], 0.0)
                nc.vector.memset(no_dst, -1.0).then_inc(s_added, PSLOTS)
                dve.wait_ge(s_last, 16)
                nc.vector.tensor_copy(last_f, last_i).then_inc(s_lastc, 1)
                for c in range(0, TROWS, 512):
                    n = min(512, TROWS - c)
                    dve.wait_ge(s_lastb, c // 512 + 1)
                    last = nc.vector.tensor_scalar(last_b[:, c:c + n], bank[c // 512][:, 0:n], 32767.0, None, ALU.min)
                last.then_inc(s_dve, 1)
                dve.wait_ge(s_dve, 1)
                dve.wait_ge(s_const, 1)
                nc.vector.tensor_scalar(is_node[:], node_id[:, 0:NW], float(N), None, ALU.is_lt)
                with dve.Fori(0, CHUNKS // 2) as i:
                    step = Steps(dve, s_dve, 1 + SEARCH * i, SEARCH)
                    for b in range(2):
                        w0 = (2 * i + b) * CW
                        for k in range(CW):
                            step(nc.vector.tensor_scalar(junk16, last_b, dyn(node_id, w0 + k, 1), 0.0, ALU.is_lt, ALU.add,
                                                         accum_out=dyn(tile_cnt, w0 + k, 1)))
                        step(nc.vector.tensor_scalar(tile_idx[:, b * CW:(b + 1) * CW], dyn(tile_cnt, w0, CW), 0.0, None, ALU.add))
                    for b in range(2):
                        w0 = (2 * i + b) * CW
                        for k in range(CW):
                            dve.wait_ge(gathered[b * CW + k], 16 * i + 16)
                        step(nc.vector.tensor_copy(found[:, b], found_i[:, b]))
                        step(nc.vector.tensor_tensor(lower[:, b], found[:, b],
                                                     dyn(node_id, w0, CW).unsqueeze(2).to_broadcast([P, CW, F]), ALU.is_lt))
                        step(nc.vector.tensor_reduce(in_tile[:, b * CW:(b + 1) * CW], lower[:, b], AX.X, ALU.add))
                        step(nc.vector.scalar_tensor_tensor(dyn(row_ptr, w0, CW), dyn(tile_cnt, w0, CW), float(P),
                                                            in_tile[:, b * CW:(b + 1) * CW], ALU.mult, ALU.add))
                    step.end()
                step = Steps(dve, s_dve, SEARCHED, MERGED - SEARCHED)
                nc.vector.memset(row_ptr[:, NW:NW + 1], float(E))
                step(nc.vector.memset(tile_cnt[:, NW:NW + 1], float(E // P)))
                dve.wait_ge(s_pe, 2)
                step(nc.vector.tensor_tensor(deg, bank[4][:, 0:NW], row_ptr[:, 0:NW], ALU.subtract))
                nc.vector.tensor_scalar(no_edges[:], deg, 0.0, None, ALU.is_equal)
                step(nc.vector.tensor_scalar(deg, deg, 1.0, None, ALU.add))
                step(nc.vector.tensor_tensor(bound[:, 0:NW], bank[5][:, 0:NW], wplus1[:, 0:NW], ALU.add))
                step(nc.vector.tensor_tensor(le, bound[:, 0:NW].unsqueeze(1).to_broadcast([P, IG, NW]),
                                             item_id[:, 0:IG].unsqueeze(2).to_broadcast([P, IG, NW]), ALU.is_le))
                step(nc.vector.tensor_reduce(item_w[:, 0:IG], le, AX.X, ALU.add))
                nc.vector.tensor_scalar(item_w128[:, 0:IG], item_w[:, 0:IG], float(P), None, ALU.mult)
                nc.vector.tensor_scalar(item_off, item_w[:, 0:IG], float(ACW), None, ALU.mult).then_inc(s_wout, 1)
                step(nc.vector.tensor_tensor(item_t, item_id[:, 0:IG], item_w[:, 0:IG], ALU.subtract))
                step.end()
                with dve.Fori(0, IG) as g:
                    step = Steps(dve, s_dve, MERGED + 2 * g, 2)
                    step(nc.vector.tensor_scalar(tcol, dyn(item_t, g, 1), 0, None, ALU.add))
                    dve.wait_ge(gathered[2 * CW + 1], 16 * g + 16)
                    dve.wait_ge(s_dlout, 16 * g + 16)
                    nc.vector.tensor_scalar(got_f[:, 1, :], got[:, 1, :].bitcast(i32), dyn(item_w128, g, 1), None,
                                            ALU.subtract).then_inc(s_dlrow, 1)
                    dve.wait_ge(s_tr, g + 1)
                    dve.wait_ge(gathered[2 * CW + 2], 16 * g + 16)
                    step(nc.vector.tensor_scalar(dyn(dl_tab, g * P, P), bank[1][:, 0:P], 0.0, None, ALU.add))
                    step.end()
                step = Steps(dve, s_dve, MERGED + 2 * IG, 1)
                dve.wait_ge(s_cnt, 1)
                step(nc.vector.reciprocal(dinv[:], deg_r))

            @block.tensor
            def _(pe):
                pe.wait_ge(s_const, 1)
                pe.wait_ge(s_weights, 16 * 22)
                nc.tensor.transpose(bank[6][:, 0:F], wload[:, 0, :], ident[:])
                nc.tensor.transpose(bank[6][:, F:2 * F], wload[:, 1, :], ident[:]).then_inc(s_pe, 1)
                pe.wait_ge(s_lastc, 1)
                for c in range(0, TROWS, 512):
                    n = min(512, TROWS - c)
                    nc.tensor.matmul(bank[c // 512][:, 0:n], ones[0:1, :], last_f[:, c:c + n], start=True, stop=True).then_inc(s_lastb, 1)
                pe.wait_ge(s_dve, SEARCHED + 1)
                nc.tensor.matmul(bank[4][:, 0:NW], shift, row_ptr[:, 0:NW], start=True, stop=False)
                nc.tensor.matmul(bank[4][:, 0:NW], wrap, row_ptr[:, 1:NW + 1], start=False, stop=True)
                nc.tensor.matmul(bank[5][:, 0:NW], first, tile_cnt[:, 1:NW + 1], start=True, stop=True).then_inc(s_pe, 1)
                with pe.Fori(0, IG) as g:
                    pe.wait_ge(s_kept, 2 * g + 1)
                    pe.wait_ge(s_dlrow, g + 1)
                    pe.wait_ge(s_dve, MERGED + 2 * g + 1)
                    pe.wait_ge(gathered[2 * CW + 2], 16 * g + 16)
                    nc.tensor.transpose(bank[0][:, 0:P], got_f[:, 0, :], ident[:])
                    nc.tensor.transpose(bank[1][:, 0:P], got_f[:, 1, :], ident[:])
                    nc.tensor.transpose(bank[0][:, 2 * P:3 * P], got[:, 2, :], ident[:]).then_inc(s_tr, 1)

        PSPLIT = [(0, 4), (4, CW)]
        std, rstd = small[:, 0, 0:CW], small[:, 1, 0:CW]

        def layernorm_steps(dve, step, w0, s_root, roots, scale, to, tmp):
            dve.sem_inc(s_tick, 1)
            for k in range(CW):
                last = nc.vector.bn_stats(stats[:, k, :], windows(xs, w0 + k).rearrange("p w f -> p (w f)"))
            step(last)
            dve.sem_inc(s_tick, 1)
            for k in range(CW):
                last = nc.vector.bn_aggr(mv[:, k, :], stats[:, k, :])
            step(last)
            dve.wait_ge(s_root, roots)
            step(nc.vector.reciprocal(rstd, std))
            step(nc.vector.tensor_tensor(rstd, rstd, dyn(scale, w0, CW), ALU.mult))
            for k in range(CW):
                last = nc.vector.tensor_scalar(tmp[:, k, :], windows(xs, w0 + k).rearrange("p w f -> p (w f)"),
                                               mv[:, k, 0:1], rstd[:, k:k + 1], ALU.subtract, ALU.mult)
            step(last)
            step(nc.vector.tensor_scalar(to, tmp, 0.0, None, ALU.max))

        LN_STEPS = 6

        def layernorm_root(s_root):
            nc.scalar.activation(std, mv[:, :, 1], ACT.Sqrt, bias=eps_ln[:]).then_inc(s_root, 1)

        def transpose_chunk(of, s_tr):
            for b, (k0, k1) in enumerate(PSPLIT):
                for k in range(k0, k1):
                    last = nc.tensor.transpose(bank[b][:, (k - k0) * F:(k - k0 + 1) * F], of[:, k, :], ident[:])
            last.then_inc(s_tr, 1)

        def keep_transposed(to, s_kept):
            for b, (k0, k1) in enumerate(PSPLIT):
                last = nc.scalar.copy(to[:, k0 * F:k1 * F], bank[b][:, 0:(k1 - k0) * F])
            last.then_inc(s_kept, 1)

        def linear_chunk(of_t, w, brow, s_lin):
            for b, (k0, k1) in enumerate(PSPLIT):
                for k in range(k0, k1):
                    o = bank[2 + b][:, (k - k0) * F:(k - k0 + 1) * F]
                    nc.tensor.matmul(o, of_t[:, k * F:(k + 1) * F], w, start=True, stop=False)
                    last = nc.tensor.matmul(o, ones[0:1, :], rows[:, brow, 0:F], start=False, stop=True)
            last.then_inc(s_lin, 1)

        def add_linear(step, w0):
            for b, (k0, k1) in enumerate(PSPLIT):
                v = windows(xs, w0 + k0, k1 - k0)
                last = nc.vector.tensor_tensor(v, v, chunk(bank[2 + b][:, 0:(k1 - k0) * F]), ALU.add)
            step(last)

        def store_table(sp, c, s_table):
            sp.sem_inc(s_tick, 1)
            sp.dma_start(node_rows(table, c), windows(acc, c * CW, CW)).then_inc(s_table, 16)

        def stage_indices(h, q):
            nc.scalar.copy(idx_stage[:, h, :], dyn(src_tab, q * HALF, HALF)).then_inc(s_staged, 1)

        def gather_rounds(pool, no, tab, slots):
            with pool.Fori(0, ROUNDS) as i:
                for h in range(2):
                    pool.wait_ge(s_staged, no * (HALVES + 2) + 2 * i + h + 1)
                    pool.sem_inc(s_tick, 1)
                    for u in range(h * HALF, (h + 1) * HALF):
                        pool.indirect_dma_start(
                            out=slots[:, u, :], out_offset=None, in_=tab,
                            in_offset=bass.IndirectOffsetOnAxis(ap=idx_stage[:, h, u % HALF:u % HALF + 1], axis=0),
                        ).then_inc(gathered[u], 16)

        def item_windows(q, engine):
            _, vals = nc.values_load_multi_w_load_instructions(
                win_tab[0:1, bass.ds(q * HALF, HALF)], engines=[engine], min_val=0, max_val=NW * ACW,
                skip_runtime_bounds_check_because="an item's window is one of the windows")
            return vals

        def pass_over_edges(no, weighted, count_weights):
            items0 = no * NI
            cols = F + 1 if count_weights else F

            with nc.Block() as block:
                @block.gpsimd
                def _(pool):
                    gather_rounds(pool, no, table, ring_n)

                @block.scalar
                def _(act):
                    stage_indices(0, 0)
                    stage_indices(1, 1)
                    with act.Fori(0, ROUNDS) as i:
                        for h in range(2):
                            act.wait_ge(s_added, PSLOTS + items0 + BODY * i + (h + 1) * HALF)
                            act.sem_inc(s_tick, 1)
                            stage_indices(h, 2 * i + h + 2)

                @block.vector
                def _(dve):
                    def build(h, q):
                        for u in range(HALF):
                            col = q * HALF + u
                            last = nc.vector.tensor_scalar(
                                onehot[:, h * HALF + u, :], iota_col[:], dyn(dl_tab, col, 1),
                                dyn(ew_tab, col, 1) if weighted else None, ALU.is_equal,
                                ALU.mult if weighted else ALU.bypass)
                        last.then_inc(s_onehot, 1)

                    build(0, 0)
                    with dve.Fori(0, ROUNDS) as i:
                        for h in range(2):
                            build(1 - h, 2 * i + h + 1)
                            at = item_windows(2 * i + h, DVE)
                            for u in range(HALF):
                                n = BODY * i + h * HALF + u
                                dve.wait_ge(s_prod, items0 + n + 1)
                                dve.wait_ge(s_added, PSLOTS + items0 + n)
                                a = acc_flat[:, bass.ds(at[u], cols)]
                                nc.vector.tensor_tensor(a, a, bank[u % PSLOTS][:, 0:cols], ALU.add).then_inc(s_added, 1)

                @block.tensor
                def _(pe):
                    with pe.Fori(0, ROUNDS) as i:
                        for h in range(2):
                            pe.wait_ge(s_onehot, no * (HALVES + 1) + 2 * i + h + 1)
                            for u in range(h * HALF, (h + 1) * HALF):
                                pe.wait_ge(s_added, items0 + BODY * i + u + 1)
                                pe.wait_ge(gathered[u], 16 * gathers[u] + 16 * i + 16)
                                o = bank[u % PSLOTS]
                                last = nc.tensor.matmul(o[:, 0:F], onehot[:, u, :], ring_n[:, u, :], start=True, stop=True)
                                if count_weights:
                                    last = nc.tensor.matmul(o[:, F:F + 1], onehot[:, u, :], dyn(ew_tab, BODY * i + u, 1),
                                                            start=True, stop=True)
                                last.then_inc(s_prod, 1)
            for u in range(BODY):
                gathers[u] += ROUNDS

        s_v, s_root, s_table, s_mask = (sem(n) for n in ("ln0_steps", "ln0_root", "ln0_table", "ln0_mask"))
        with nc.Block() as block:
            @block.vector
            def _(dve):
                nc.vector.tensor_tensor(deg_r, dinv[:], is_node[:], ALU.mult).then_inc(s_mask, 1)
                dve.wait_ge(s_mask, 1)
                with dve.Fori(0, CHUNKS) as c:
                    step = Steps(dve, s_v, LN_STEPS * c, LN_STEPS)
                    layernorm_steps(dve, step, c * CW, s_root, c + 1, deg_r, windows(acc, c * CW, CW), chunk(work[:, 0, :]))
                    step.end()

            @block.scalar
            def _(act):
                with act.Fori(0, CHUNKS) as c:
                    act.wait_ge(s_v, LN_STEPS * c + 2)
                    layernorm_root(s_root)

            @block.sync
            def _(sp):
                with sp.Fori(0, CHUNKS) as c:
                    sp.wait_ge(s_v, LN_STEPS * (c + 1))
                    store_table(sp, c, s_table)
                sp.wait_ge(s_table, 16 * CHUNKS)

        pass_over_edges(0, weighted=False, count_weights=True)

        s_v, s_tr, s_kept, s_hid, s_h1, s_lin, s_table, s_root = (sem(n) for n in (
            "mlp_steps", "mlp_transposed", "mlp_kept", "mlp_hidden", "mlp_relu", "mlp_out", "mlp_table", "mlp_root"))
        HC = CC // 2
        with nc.Block() as block:
            @block.vector
            def _(dve):
                step = Steps(dve, s_v, 0, 4)
                step(nc.vector.tensor_scalar(deg, acc[:, 0:NW, F], TINY, None, ALU.max))
                dve.wait_ge(s_root, 1)
                step(nc.vector.reciprocal(dinv2[:], deg_r))
                step(nc.vector.tensor_scalar(deg, acc[:, 0:NW, F], 0.0, None, ALU.is_gt))
                step(nc.vector.tensor_tensor(dinv2[:], dinv2[:], deg, ALU.mult))
                step.end()
                with dve.Fori(0, CHUNKS) as c:
                    step = Steps(dve, s_v, 4 + 2 * c, 2)
                    y = chunk(work[:, 0, :])
                    step(nc.vector.tensor_tensor(y, windows(acc, c * CW, CW), over_f(dyn(dinv, c * CW, CW)), ALU.mult))
                    dve.wait_ge(s_lin, c + 1)
                    for b, (k0, k1) in enumerate(PSPLIT):
                        last = nc.vector.tensor_tensor(windows(acc, c * CW + k0, k1 - k0), chunk(bank[6 + b][:, 0:(k1 - k0) * F]),
                                                       over_f(dyn(dinv, c * CW + k0, k1 - k0), k1 - k0), ALU.mult)
                    step(last)
                    step.end()

            @block.tensor
            def _(pe):
                with pe.Fori(0, CHUNKS) as c:
                    pe.wait_ge(s_v, 4 + 2 * c + 1)
                    transpose_chunk(chunk(work[:, 0, :]), s_tr)
                    pe.wait_ge(s_kept, c + 1)
                    for m in range(HM):
                        for j in range(2):
                            last = nc.tensor.matmul(bank[2 + 2 * m + j][:, 0:HC], w1[:, m * P:(m + 1) * P],
                                                    work[:, 1, j * HC:(j + 1) * HC], start=True, stop=True)
                    last.then_inc(s_hid, 1)
                    pe.wait_ge(s_h1, c + 1)
                    for b, (k0, k1) in enumerate(PSPLIT):
                        for k in range(k0, k1):
                            for m in range(HM):
                                last = nc.tensor.matmul(bank[6 + b][:, (k - k0) * F:(k - k0 + 1) * F],
                                                        work[:, 2 + m, k * F:(k + 1) * F], w2[:, m, :],
                                                        start=(m == 0), stop=(m == HM - 1))
                    last.then_inc(s_lin, 1)

            @block.scalar
            def _(act):
                act.wait_ge(s_v, 1)
                nc.scalar.activation(deg_r, deg, ACT.Sqrt).then_inc(s_root, 1)
                with act.Fori(0, CHUNKS) as c:
                    act.wait_ge(s_tr, c + 1)
                    keep_transposed(work[:, 1, :], s_kept)
                    act.wait_ge(s_hid, c + 1)
                    for m in range(HM):
                        for j in range(2):
                            last = nc.scalar.activation(work[:, 2 + m, j * HC:(j + 1) * HC], bank[2 + 2 * m + j][:, 0:HC],
                                                        ACT.Relu, bias=b1c[:, m:m + 1])
                    last.then_inc(s_h1, 1)

            @block.sync
            def _(sp):
                with sp.Fori(0, CHUNKS) as c:
                    sp.wait_ge(s_v, 4 + 2 * c + 2)
                    store_table(sp, c, s_table)
                sp.wait_ge(s_table, 16 * CHUNKS)

        pass_over_edges(1, weighted=False, count_weights=False)

        s_v, s_root, s_table, s_tot, s_wide, s_zero = (sem(n) for n in (
            "l1_steps", "l1_root", "l1_table", "l1_total", "l1_wide", "l1_zero"))
        zero_row = work[:, 3, 0:F]
        L1_STEPS = 3 + LN_STEPS
        with nc.Block() as block:
            @block.vector
            def _(dve):
                dve.wait_ge(s_wide, 1)
                step = Steps(dve, s_v, 0, 1)
                step(nc.vector.tensor_copy(wide[:, 0, 0:F], bank[1][:, 0:F]))
                with dve.Fori(0, CHUNKS) as c:
                    step = Steps(dve, s_v, 1 + L1_STEPS * c, L1_STEPS)
                    y, xc = chunk(work[:, 0, :]), windows(xs, c * CW, CW)
                    step(nc.vector.tensor_tensor(y, windows(acc, c * CW, CW), over_f(dyn(dinv, c * CW, CW)), ALU.mult))
                    step(nc.vector.tensor_tensor(y, y, over_w(wide[:, 0, 0:F]), ALU.add))
                    step(nc.vector.tensor_tensor(xc, xc, y, ALU.add))
                    layernorm_steps(dve, step, c * CW, s_root, c + 1, is_node, windows(acc, c * CW, CW), y)
                    step.end()
                dve.wait_ge(s_tot, CHUNKS + 1)
                dve.wait_ge(s_table, 16 * CHUNKS)
                nc.vector.tensor_copy(wide[:, 0, 0:F], bank[0][:, 0:F])
                nc.vector.memset(acc[:, 0:NW // 2, 0:F], 0.0)

            @block.gpsimd
            def _(pool):
                nc.gpsimd.memset(zero_row, 0.0).then_inc(s_zero, 1)
                pool.wait_ge(s_tot, CHUNKS + 1)
                pool.wait_ge(s_table, 16 * CHUNKS)
                nc.gpsimd.memset(acc[:, NW // 2:NW, 0:F], 0.0)

            @block.tensor
            def _(pe):
                nc.tensor.matmul(bank[1][:, 0:F], ones[0:1, :], rows[:, B2, 0:F], start=True, stop=True).then_inc(s_wide, 1)
                pe.wait_ge(s_zero, 1)
                nc.tensor.matmul(bank[0][:, 0:F], ones[:], zero_row, start=True, stop=False, skip_group_check=True)
                with pe.Fori(0, CHUNKS) as c:
                    pe.wait_ge(s_v, 1 + L1_STEPS * (c + 1))
                    for k in range(CW):
                        last = nc.tensor.matmul(bank[0][:, 0:F], ones[:], windows(acc, c * CW + k).rearrange("p w f -> p (w f)"),
                                                start=False, stop=False, skip_group_check=True)
                    last.then_inc(s_tot, 1)
                nc.tensor.matmul(bank[0][:, 0:F], ones[:], zero_row, start=False, stop=True, skip_group_check=True).then_inc(s_tot, 1)

            @block.scalar
            def _(act):
                with act.Fori(0, CHUNKS) as c:
                    act.wait_ge(s_v, 1 + L1_STEPS * c + 3 + 2)
                    layernorm_root(s_root)

            @block.sync
            def _(sp):
                with sp.Fori(0, CHUNKS) as c:
                    sp.wait_ge(s_v, 1 + L1_STEPS * (c + 1))
                    store_table(sp, c, s_table)
                sp.wait_ge(s_table, 16 * CHUNKS)

        pass_over_edges(2, weighted=False, count_weights=False)

        s_v, s_root, s_table, s_sq, s_norm, s_tr, s_kept, s_lin, s_mask = (sem(n) for n in (
            "l2_steps", "l2_root", "l2_table", "l2_square", "l2_norm", "l2_transposed", "l2_kept", "l2_linear", "l2_mask"))
        sumsq, norm = small[:, 2, 0:CW], small[:, 3, 0:CW]
        L2_STEPS = 6 + LN_STEPS
        with nc.Block() as block:
            @block.vector
            def _(dve):
                nc.vector.tensor_tensor(deg_r, dinv2[:], is_node[:], ALU.mult).then_inc(s_mask, 1)
                dve.wait_ge(s_mask, 1)
                with dve.Fori(0, CHUNKS) as c:
                    step = Steps(dve, s_v, L2_STEPS * c, L2_STEPS)
                    hn = chunk(work[:, 0, :])
                    step(nc.vector.tensor_tensor(hn, over_w(wide[:, 0, 0:F]), windows(acc, c * CW, CW), ALU.subtract))
                    dve.wait_ge(s_sq, c + 1)
                    step(nc.vector.tensor_reduce(sumsq, chunk(work[:, 1, :]), AX.X, ALU.add))
                    dve.wait_ge(s_norm, c + 1)
                    step(nc.vector.tensor_scalar(norm, norm, NORM_EPS, None, ALU.max))
                    step(nc.vector.reciprocal(norm, norm))
                    step(nc.vector.tensor_tensor(hn, hn, over_f(norm), ALU.mult))
                    dve.wait_ge(s_lin, c + 1)
                    add_linear(step, c * CW)
                    layernorm_steps(dve, step, c * CW, s_root, c + 1, deg_r, windows(acc, c * CW, CW), hn)
                    step.end()

            @block.tensor
            def _(pe):
                with pe.Fori(0, CHUNKS) as c:
                    pe.wait_ge(s_v, L2_STEPS * c + 5)
                    transpose_chunk(chunk(work[:, 0, :]), s_tr)
                    pe.wait_ge(s_kept, c + 1)
                    linear_chunk(work[:, 2, :], w_l1[:], BL1, s_lin)

            @block.scalar
            def _(act):
                with act.Fori(0, CHUNKS) as c:
                    act.wait_ge(s_v, L2_STEPS * c + 1)
                    nc.scalar.activation(work[:, 1, :], work[:, 0, :], ACT.Square).then_inc(s_sq, 1)
                    act.wait_ge(s_v, L2_STEPS * c + 2)
                    nc.scalar.activation(norm, sumsq, ACT.Sqrt).then_inc(s_norm, 1)
                    act.wait_ge(s_tr, c + 1)
                    keep_transposed(work[:, 2, :], s_kept)
                    act.wait_ge(s_v, L2_STEPS * c + 6 + 2)
                    layernorm_root(s_root)

            @block.sync
            def _(sp):
                with sp.Fori(0, CHUNKS) as c:
                    sp.wait_ge(s_v, L2_STEPS * (c + 1))
                    store_table(sp, c, s_table)
                sp.wait_ge(s_table, 16 * CHUNKS)

        pass_over_edges(3, weighted=True, count_weights=False)

        s_v, s_root, s_table, s_tr, s_kept, s_lin, s_proj, s_pkept, s_zero = (sem(n) for n in (
            "l3_steps", "l3_root", "l3_table", "l3_transposed", "l3_kept", "l3_linear", "l3_projected", "l3_pkept", "l3_zero"))
        L3_STEPS = 4 + LN_STEPS
        ZSPLIT = [(k, min(k + 3, CW)) for k in range(0, CW, 3)]
        pstage = ring[:, 0:CW, :]
        with nc.Block() as block:
            @block.vector
            def _(dve):
                with dve.Fori(0, CHUNKS) as c:
                    step = Steps(dve, s_v, L3_STEPS * c, L3_STEPS)
                    y, h, xc = chunk(work[:, 0, :]), chunk(work[:, 2, :]), windows(xs, c * CW, CW)
                    step(nc.vector.tensor_tensor(y, windows(acc, c * CW, CW), over_f(dyn(dinv2, c * CW, CW)), ALU.mult))
                    dve.wait_ge(s_lin, c + 1)
                    add_linear(step, c * CW)
                    layernorm_steps(dve, step, c * CW, s_root, c + 1, is_node, h, y)
                    step(nc.vector.tensor_tensor(xc, xc, h, ALU.add))
                    dve.wait_ge(s_proj, c + 1)
                    for b, (k0, k1) in enumerate(ZSPLIT):
                        last = nc.vector.tensor_scalar(acc[:, bass.ds(c * CW + k0, k1 - k0), 0:SCW],
                                                       bank[5 + b][:, 0:(k1 - k0) * SCW].rearrange("p (w f) -> p w f", f=SCW),
                                                       0.0, None, ALU.add)
                    step(last)
                    step.end()

            @block.tensor
            def _(pe):
                with pe.Fori(0, CHUNKS) as c:
                    pe.wait_ge(s_v, L3_STEPS * c + 1)
                    transpose_chunk(chunk(work[:, 0, :]), s_tr)
                    pe.wait_ge(s_kept, 2 * c + 1)
                    pe.wait_ge(s_pkept, c + 1)
                    linear_chunk(work[:, 1, :], w_l2[:], BL2, s_lin)
                    pe.wait_ge(s_v, L3_STEPS * c + 2 + LN_STEPS)
                    transpose_chunk(chunk(work[:, 2, :]), s_tr)
                    pe.wait_ge(s_kept, 2 * c + 2)
                    for part in range(2):
                        for b, (k0, k1) in enumerate(ZSPLIT):
                            for k in range(k0, k1):
                                last = nc.tensor.matmul(bank[2 + 3 * part + b][:, (k - k0) * SCW:(k - k0 + 1) * SCW],
                                                        work[:, 1, k * F:(k + 1) * F], w_z[:, part, :], start=True, stop=True)
                    last.then_inc(s_proj, 1)

            @block.scalar
            def _(act):
                act.sem_inc(s_pkept, 1)
                with act.Fori(0, CHUNKS) as c:
                    act.wait_ge(s_tr, 2 * c + 1)
                    keep_transposed(work[:, 1, :], s_kept)
                    act.wait_ge(s_v, L3_STEPS * c + 2 + 2)
                    layernorm_root(s_root)
                    act.wait_ge(s_tr, 2 * c + 2)
                    keep_transposed(work[:, 1, :], s_kept)
                    act.wait_ge(s_proj, c + 1)
                    act.wait_ge(s_table, 16 * c + 16)
                    for b, (k0, k1) in enumerate(ZSPLIT):
                        nc.scalar.copy(pstage[:, k0:k1, 0:SCW], bank[2 + b][:, 0:(k1 - k0) * SCW].rearrange("p (w f) -> p w f", f=SCW))
                    nc.scalar.copy(pstage[:, :, SCW], dyn(node_w, c * CW, CW)).then_inc(s_pkept, 1)

            @block.sync
            def _(sp):
                sp.sem_inc(s_table, 16)
                with sp.Fori(0, CHUNKS) as c:
                    sp.wait_ge(s_pkept, c + 2)
                    sp.sem_inc(s_tick, 1)
                    sp.dma_start(node_rows(ptable, c), pstage).then_inc(s_table, 16)
                sp.wait_ge(s_table, 16 * CHUNKS + 16)

        s_dl, s_in, s_sq, s_stat, s_zout, s_zero = (sem(n) for n in (
            "z_dst", "z_in_window", "z_square", "z_stat", "z_out", "z_zero"))
        no = 4
        items0 = no * NI
        dl_wide = work[:].rearrange("p a c -> p (a c)")[:, 0:HALF * P]
        onehot_t = onehot[:].rearrange("p (h u) f -> p h (u f)", h=2)
        z_stats = bank[7]
        zero_stats = work[:].rearrange("p a c -> p (a c)")[:, HALF * P:HALF * P + ACW + SCW]
        in_win = sc16[:, 0:2, :]
        low = sc16[:, 2, :]
        with nc.Block() as block:
            @block.gpsimd
            def _(pool):
                nc.gpsimd.memset(zero_stats, 0.0).then_inc(s_zero, 1)
                gather_rounds(pool, no, ptable, ring)

            @block.sync
            def _(sp):
                def load_dst(q):
                    sp.sem_inc(s_tick, 1)
                    sp.dma_start(dl_wide, dl_rows[bass.ds(q * HALF, HALF), :].rearrange("i e -> (i e)").partition_broadcast(P)).then_inc(s_dl, 16)

                sp.sem_inc(s_zout, 16)
                load_dst(0)
                with sp.Fori(0, ROUNDS) as i:
                    for h in range(2):
                        q = 2 * i + h
                        sp.wait_ge(s_onehot, no * (HALVES + 1) + q + 1)
                        load_dst(q + 1)
                        sp.wait_ge(s_added, PSLOTS + items0 + (q + 1) * HALF)
                        sp.sem_inc(s_tick, 1)
                        sp.dma_start(zrows[bass.ds(q, 1), :, :].rearrange("o p (u f) -> p (o u) f", f=ACW), zbuf[:, :, 0:ACW]).then_inc(s_zout, 16)
                sp.wait_ge(s_zout, 16 * HALVES + 16)
                sp.wait_ge(s_dl, 16 * (HALVES + 1))

            @block.vector
            def _(dve):
                def build(h, q):
                    dve.wait_ge(s_dl, 16 * (q + 1))
                    nc.vector.tensor_scalar(onehot_t[:, h, :], dl_wide, iota_row[:], None, ALU.is_equal)
                    d = dyn(dl_tab, q * HALF, HALF)
                    nc.vector.tensor_scalar(low, d, 0.0, None, ALU.is_ge).then_inc(s_in, 1)
                    dve.wait_ge(s_in, q + 1)
                    nc.vector.scalar_tensor_tensor(in_win[:, h, :], d, float(P), low, ALU.is_lt, ALU.mult).then_inc(s_onehot, 1)

                build(0, 0)
                with dve.Fori(0, ROUNDS) as i:
                    for h in range(2):
                        q = 2 * i + h
                        dve.wait_ge(s_stat, q * HALF + 1)
                        build(1 - h, q + 1)
                        dve.wait_ge(s_zout, 16 * q + 16)
                        for u in range(HALF):
                            n = BODY * i + h * HALF + u
                            s = h * HALF + u
                            dve.wait_ge(s_prod, items0 + n + 1)
                            dve.wait_ge(gathered[s], 16 * gathers[s] + 16 * i + 16)
                            nc.vector.tensor_tensor(zbuf[:, u, 0:ACW], bank[u % PSLOTS][:, 0:ACW], ring[:, s, :], ALU.add).then_inc(s_added, 1)

            @block.tensor
            def _(pe):
                pe.wait_ge(s_zero, 1)
                nc.tensor.matmul(z_stats[0:1, 0:ACW + SCW], ones[:, 0:1], zero_stats, start=True, stop=False, skip_group_check=True).then_inc(s_stat, 1)

                def summed(i, h, u):
                    pe.wait_ge(s_sq, BODY * i + h * HALF + u + 1)
                    nc.tensor.matmul(z_stats[0:1, 0:ACW + SCW], in_win[:, h, u:u + 1], zbuf[:, u, :],
                                     start=False, stop=False, skip_group_check=True).then_inc(s_stat, 1)

                with pe.Fori(0, ROUNDS) as i:
                    for h in range(2):
                        pe.wait_ge(s_onehot, no * (HALVES + 1) + 2 * i + h + 1)
                        at = item_windows(2 * i + h, PE)
                        for u in range(HALF):
                            pe.wait_ge(s_added, items0 + BODY * i + h * HALF + u + 1)
                            nc.tensor.matmul(bank[u % PSLOTS][:, 0:ACW], onehot_t[:, h, u * P:(u + 1) * P],
                                             acc_flat[:, bass.ds(at[u], ACW)], start=True, stop=True).then_inc(s_prod, 1)
                            if u >= 2:
                                summed(i, h, u - 2)
                        for u in range(HALF - 2, HALF):
                            summed(i, h, u)
                nc.tensor.matmul(z_stats[0:1, 0:ACW + SCW], ones[:, 0:1], zero_stats, start=False, stop=True, skip_group_check=True)

            @block.scalar
            def _(act):
                stage_indices(0, 0)
                stage_indices(1, 1)
                with act.Fori(0, ROUNDS) as i:
                    for h in range(2):
                        for u in range(HALF):
                            act.wait_ge(s_added, PSLOTS + items0 + BODY * i + h * HALF + u + 1)
                            nc.scalar.activation(zbuf[:, u, ACW:ACW + SCW], zbuf[:, u, 0:SCW], ACT.Square).then_inc(s_sq, 1)
                        stage_indices(h, 2 * i + h + 2)
        for u in range(BODY):
            gathers[u] += ROUNDS

        s_v, s_root, s_wide = (sem(n) for n in ("bn_steps", "bn_root", "bn_wide"))
        mean, var, scale_r, shift_r = (rows[:, k, :] for k in (RT0, RT1, RT2, RT3))
        with nc.Block() as block:
            @block.vector
            def _(dve):
                step = Steps(dve, s_v, 0, 12)
                step(nc.vector.tensor_scalar(mean, z_stats[0:1, 0:SCW], 1.0 / E, None, ALU.mult))
                step(nc.vector.tensor_scalar(var, z_stats[0:1, ACW:ACW + SCW], 1.0 / E, None, ALU.mult))
                step(nc.vector.tensor_tensor(scale_r, mean, mean, ALU.mult))
                step(nc.vector.tensor_tensor(var, var, scale_r, ALU.subtract))
                step(nc.vector.tensor_scalar(var, var, 0.0, None, ALU.max))
                dve.wait_ge(s_root, 1)
                step(nc.vector.reciprocal(var, var))
                step(nc.vector.tensor_tensor(scale_r, var, rows[:, GAMMA, :], ALU.mult))
                step(nc.vector.tensor_tensor(mean, mean, rows[:, BGF, :], ALU.add))
                step(nc.vector.tensor_tensor(shift_r, rows[:, BGF, :], mean, ALU.subtract))
                step(nc.vector.tensor_tensor(shift_r, shift_r, scale_r, ALU.mult))
                step(nc.vector.tensor_tensor(shift_r, shift_r, rows[:, BETA, :], ALU.add))
                dve.wait_ge(s_wide, 1)
                step(nc.vector.tensor_copy(wide[:, 0:2, :], bank[6][:, 0:2 * SCW].rearrange("p (a f) -> p a f", a=2)))
                step.end()
                nc.vector.memset(acc[:, 0:NW // 2, 0:SCW], 0.0)
                nc.vector.memset(zbuf[:, :, F:SCW], 1.0)

            @block.gpsimd
            def _(pool):
                nc.gpsimd.memset(acc[:, NW // 2:NW + 1, 0:SCW], 0.0)

            @block.scalar
            def _(act):
                act.wait_ge(s_v, 5)
                nc.scalar.activation(var, var, ACT.Sqrt, bias=eps_ln[0:1, :]).then_inc(s_root, 1)

            @block.tensor
            def _(pe):
                pe.wait_ge(s_v, 11)
                nc.tensor.matmul(bank[6][:, 0:2 * SCW], ones[0:1, :], rows[:, RT2:RT3 + 1, :].rearrange("p a f -> p (a f)"),
                                 start=True, stop=True).then_inc(s_wide, 1)

        s_z = [sem(f"msg_z{h}") for h in range(2)]
        s_v, s_scaled, s_th, s_ex, s_t = (sem(n) for n in (
            "msg_steps", "msg_scaled", "msg_tanh_score", "msg_exp", "msg_tanh"))
        no = 5
        items0 = no * NI
        z_in = ring[:].rearrange("p (h u) f -> p h u f", h=2)
        zn = work[:].rearrange("p a c -> p (a c)")[:, 0:HALF * F].rearrange("p (u f) -> p u f", f=F)
        t = zbuf[:, :, ACW:ACW + F]
        M_STEPS = 5
        oh0 = no * (HALVES + 1)
        with nc.Block() as block:
            @block.sync
            def _(sp):
                def load_z(h, q):
                    sp.sem_inc(s_tick, 1)
                    sp.dma_start(z_in[:, h], zrows[bass.ds(q, 1), :, :].rearrange("o p (u f) -> p (o u) f", f=ACW)).then_inc(s_z[h], 16)

                load_z(0, 0)
                load_z(1, 1)
                with sp.Fori(0, ROUNDS - 1) as i:
                    for h in range(2):
                        sp.wait_ge(s_v, 1 + M_STEPS * (2 * i + h) + M_STEPS)
                        sp.sem_inc(s_tick, 1)
                        sp.wait_ge(s_scaled, 2 * i + h + 1)
                        load_z(h, 2 * i + h + 2)

            @block.gpsimd
            def _(pool):
                with pool.Fori(0, ROUNDS) as i:
                    for h in range(2):
                        pool.wait_ge(s_v, 1 + M_STEPS * (2 * i + h))
                        pool.sem_inc(s_tick, 1)
                        pool.wait_ge(s_z[h], 16 * i + 16)
                        nc.gpsimd.tensor_tensor(zn, z_in[:, h, :, 0:F], over_w(wide[:, 0, 0:F], HALF), ALU.mult).then_inc(s_scaled, 1)

            @block.scalar
            def _(act):
                with act.Fori(0, ROUNDS) as i:
                    for h in range(2):
                        q = 2 * i + h
                        act.wait_ge(s_v, M_STEPS * q + 2)
                        nc.scalar.activation(sc16[:, 1, :], sc16[:, 0, :], ACT.Tanh, scale=0.5).then_inc(s_th, 1)
                        act.wait_ge(s_v, M_STEPS * q + 3)
                        nc.scalar.activation(sc16[:, 3, :], sc16[:, 2, :], ACT.Exp, scale=0.5).then_inc(s_ex, 1)
                        act.wait_ge(s_v, M_STEPS * q + 5)
                        nc.scalar.activation(t, zn, ACT.Tanh, scale=0.5).then_inc(s_t, 1)

            @block.vector
            def _(dve):
                dve.sem_inc(s_v, 1)
                with dve.Fori(0, ROUNDS) as i:
                    for h in range(2):
                        q = 2 * i + h
                        step = Steps(dve, s_v, 1 + M_STEPS * q, M_STEPS)
                        dve.wait_ge(s_z[h], 16 * i + 16)
                        step(nc.vector.tensor_scalar(sc16[:, 0, :], z_in[:, h, :, F], wide[:, 0, F:SCW], wide[:, 1, F:SCW], ALU.mult, ALU.add))
                        dve.wait_ge(s_th, q + 1)
                        step(nc.vector.scalar_tensor_tensor(sc16[:, 2, :], sc16[:, 1, :], 1.0, sc16[:, 0, :], ALU.add, ALU.mult))
                        dve.wait_ge(s_ex, q + 1)
                        step(nc.vector.tensor_tensor(sc16[:, 4, :], sc16[:, 3, :], z_in[:, h, :, SCW], ALU.mult))
                        dve.wait_ge(s_scaled, q + 1)
                        step(nc.vector.tensor_tensor(zn, zn, over_w(wide[:, 1, 0:F], HALF), ALU.add))
                        for u in range(HALF):
                            last = nc.vector.tensor_scalar(onehot[:, h * HALF + u, :], iota_col[:], dyn(dl_tab, q * HALF + u, 1),
                                                           sc16[:, 4, u:u + 1], ALU.is_equal, ALU.mult)
                        last.then_inc(s_onehot, 1)
                        dve.wait_ge(s_t, q + 1)
                        step(nc.vector.scalar_tensor_tensor(zbuf[:, :, 0:F], t, 1.0, zn, ALU.add, ALU.mult))
                        step.end()
                        at = item_windows(q, DVE)
                        for u in range(HALF):
                            n = BODY * i + h * HALF + u
                            dve.wait_ge(s_prod, items0 + n + 1)
                            dve.wait_ge(s_added, PSLOTS + items0 + n)
                            a = acc_flat[:, bass.ds(at[u], SCW)]
                            nc.vector.tensor_tensor(a, a, bank[u % PSLOTS][:, 0:SCW], ALU.add).then_inc(s_added, 1)

            @block.tensor
            def _(pe):
                with pe.Fori(0, ROUNDS) as i:
                    for h in range(2):
                        q = 2 * i + h
                        pe.wait_ge(s_onehot, oh0 + q + 1)
                        pe.wait_ge(s_v, M_STEPS * q + 6)
                        for u in range(HALF):
                            pe.wait_ge(s_added, items0 + BODY * i + h * HALF + u + 1)
                            nc.tensor.matmul(bank[u % PSLOTS][:, 0:SCW], onehot[:, h * HALF + u, :], zbuf[:, u, 0:SCW],
                                             start=True, stop=True).then_inc(s_prod, 1)

        s_v, s_tot, s_sq, s_root, s_wide, s_zero, s_out = (sem(n) for n in (
            "end_steps", "end_total", "end_square", "end_root", "end_wide", "end_zero", "end_out"))
        TOP = CHUNKS * 4
        MID = TOP + 1
        LOW = MID + CHUNKS * 2
        with nc.Block() as block:
            @block.vector
            def _(dve):
                with dve.Fori(0, CHUNKS) as c:
                    step = Steps(dve, s_v, 4 * c, 4)
                    hc = windows(acc, c * CW, CW)
                    den = small[:, 0, 0:CW]
                    step(nc.vector.tensor_tensor(den, acc[:, bass.ds(c * CW, CW), F], dyn(no_edges, c * CW, CW), ALU.add))
                    step(nc.vector.reciprocal(den, den))
                    step(nc.vector.tensor_scalar(den, den, 0.5, None, ALU.mult))
                    step(nc.vector.tensor_tensor(hc, hc, over_f(den), ALU.mult))
                    step.end()
                step = Steps(dve, s_v, TOP, 1)
                dve.wait_ge(s_tot, CHUNKS + 1)
                step(nc.vector.tensor_scalar(wide[:, 0, 0:F], bank[0][:, 0:F], 1.0 / N, None, ALU.mult))
                with dve.Fori(0, CHUNKS) as c:
                    step = Steps(dve, s_v, MID + 2 * c, 2)
                    hc = windows(acc, c * CW, CW)
                    step(nc.vector.tensor_tensor(hc, hc, over_w(wide[:, 0, 0:F]), ALU.subtract))
                    step(nc.vector.tensor_tensor(hc, hc, over_f(dyn(is_node, c * CW, CW)), ALU.mult))
                    step.end()
                step = Steps(dve, s_v, LOW, 4)
                dve.wait_ge(s_tot, 2 * CHUNKS + 2)
                step(nc.vector.tensor_scalar(wide[:, 1, 0:F], bank[1][:, 0:F], 1.0 / N, None, ALU.mult))
                dve.wait_ge(s_root, 1)
                step(nc.vector.reciprocal(wide[:, 1, 0:F], wide[:, 1, 0:F]))
                dve.wait_ge(s_wide, 1)
                step(nc.vector.tensor_tensor(wide[:, 1, 0:F], wide[:, 1, 0:F], bank[2][:, 0:F], ALU.mult))
                step(nc.vector.tensor_copy(wide[:, 2, 0:F], bank[2][:, F:2 * F]))
                step.end()
                with dve.Fori(0, CHUNKS) as c:
                    step = Steps(dve, s_v, LOW + 4 + 3 * c, 3)
                    hc, xc = windows(acc, c * CW, CW), windows(xs, c * CW, CW)
                    step(nc.vector.tensor_tensor(hc, hc, over_w(wide[:, 1, 0:F]), ALU.mult))
                    step(nc.vector.tensor_tensor(hc, hc, over_w(wide[:, 2, 0:F]), ALU.add))
                    step(nc.vector.tensor_tensor(xc, xc, hc, ALU.add))
                    step.end()

            @block.gpsimd
            def _(pool):
                nc.gpsimd.memset(zero_row, 0.0).then_inc(s_zero, 1)

            @block.scalar
            def _(act):
                with act.Fori(0, CHUNKS) as c:
                    act.wait_ge(s_v, MID + 2 * c + 2)
                    act.sem_inc(s_tick, 1)
                    act.wait_ge(s_tot, CHUNKS + 1 + c)
                    act.sem_inc(s_tick, 1)
                    nc.scalar.activation(chunk(work[:, 0, :]), windows(acc, c * CW, CW), ACT.Square).then_inc(s_sq, 1)
                act.wait_ge(s_v, LOW + 1)
                nc.scalar.activation(wide[:, 1, 0:F], wide[:, 1, 0:F], ACT.Sqrt, bias=eps_ln[:]).then_inc(s_root, 1)

            @block.tensor
            def _(pe):
                for b in range(2):
                    last = nc.tensor.matmul(bank[2][:, b * F:(b + 1) * F], ones[0:1, :], rows[:, NGAMMA + b, 0:F], start=True, stop=True)
                last.then_inc(s_wide, 1)
                pe.wait_ge(s_zero, 1)
                for b in range(2):
                    nc.tensor.matmul(bank[b][:, 0:F], ones[:], zero_row, start=True, stop=False, skip_group_check=True)
                    with pe.Fori(0, CHUNKS) as c:
                        if b == 0:
                            pe.wait_ge(s_v, 4 * c + 4)
                        else:
                            pe.wait_ge(s_sq, c + 1)
                        for k in range(CW):
                            of = windows(acc, c * CW + k).rearrange("p w f -> p (w f)") if b == 0 else work[:, 0, k * F:(k + 1) * F]
                            last = nc.tensor.matmul(bank[b][:, 0:F], ones[:], of, start=False, stop=False, skip_group_check=True)
                        last.then_inc(s_tot, 1)
                    nc.tensor.matmul(bank[b][:, 0:F], ones[:], zero_row, start=False, stop=True, skip_group_check=True).then_inc(s_tot, 1)

            @block.sync
            def _(sp):
                with sp.Fori(0, CHUNKS - 1) as c:
                    sp.wait_ge(s_v, LOW + 4 + 3 * c + 3)
                    sp.sem_inc(s_tick, 1)
                    sp.dma_start(node_rows(out, c), windows(xs, c * CW, CW)).then_inc(s_out, 16)
                sp.wait_ge(s_v, LOW + 4 + 3 * CHUNKS)
                w0 = NW - CW
                sp.dma_start(out[w0 * P:(NW - 1) * P, :].rearrange("(w p) f -> p w f", p=P), xs[:, w0:NW - 1, :]).then_inc(s_out, 16)
                sp.dma_start(out[(NW - 1) * P:N, :], xs[0:TAIL, NW - 1, :]).then_inc(s_out, 16)
                sp.wait_ge(s_out, 16 * (CHUNKS + 1))


_INS = ["x", "src", "dst", "edge_weight", "node_vec1", "L0_gnn_W1", "L0_gnn_b1", "L0_gnn_W2", "L0_gnn_b2", "L1_gnn_W", "L1_gnn_b",
        "L2_gnn_W", "L2_gnn_b", "L3_gnn_Wf", "L3_gnn_bf", "L3_gnn_f_gamma", "L3_gnn_f_beta", "L3_gnn_Wg", "L3_gnn_bg",
        "L3_gnn_g_gamma", "L3_gnn_g_beta", "L3_gnn_n_gamma", "L3_gnn_n_beta"]


def kernel(**inputs):
    import numpy as np
    import concourse.bacc as bacc
    from concourse.bass_utils import run_bass_kernel_spmd

    nc = bacc.Bacc("TRN2", target_bir_lowering=False, num_devices=1)
    arrays, args = {}, []
    for name in _INS:
        a = np.ascontiguousarray(inputs[name])
        arrays[f"in_{name}"] = a
        args.append(nc.dram_tensor(f"in_{name}", a.shape, mybir.dt.from_np(a.dtype), kind="ExternalInput").ap())
    out = nc.dram_tensor("out", arrays["in_x"].shape, mybir.dt.float32, kind="ExternalOutput").ap()
    gnn_kernel(nc, *args, out)
    r = run_bass_kernel_spmd(nc, [arrays], core_ids=[0])
    return r.results[0]["out"]
```
